# Optimizing a Trainium2 kernel written in Bass

```python
import numpy as np
import jax
import jax.numpy as jnp

def _softmax(x, axis=-1):
    return jax.nn.softmax(x, axis=axis)

def _gelu(x):
    return jax.nn.gelu(x, approximate=True)

def _silu(x):
    return jax.nn.silu(x)

def _sigmoid(x):
    return jax.nn.sigmoid(x)

def _layernorm(x, axis=-1, eps=1e-05):
    m = jnp.mean(x, axis=axis, keepdims=True)
    v = jnp.var(x, axis=axis, keepdims=True)
    return (x - m) / jnp.sqrt(v + eps)

def _scatter_add(tgt, idx, src, axis=0):
    return tgt.at[idx].add(src)

def _segment_sum(src, seg, n):
    return jax.ops.segment_sum(src, seg, n)
kernel_name = 'mk_gnn_preln_d1_gnn_r8_0f360e'

def setup_inputs(seed: int=0):
    np.random.seed(seed)
    _w = jnp.asarray

    def _rec_inputs():
        import jax
        import jax.numpy as jnp
        _gk = jax.random.key(seed)
        x = -0.0009044 + 1 * jax.random.normal(jax.random.fold_in(_gk, 1), (12500, 16), jnp.float32)
        src = jax.random.randint(jax.random.fold_in(_gk, 2), (400000,), 0, 12500, jnp.int32)
        dst = jnp.minimum((12500 * jax.random.uniform(jax.random.fold_in(_gk, 3), (400000,)) ** 2.0).astype(jnp.int32), 99999)
        _o = jnp.argsort(dst, stable=True)
        src = src[_o]
        dst = dst[_o]
        edge_attr_64 = -2.32664e-05 + 0.999985 * jax.random.normal(jax.random.fold_in(_gk, 12), (400000, 64), jnp.float32)
        edge_weight1 = jax.random.uniform(jax.random.fold_in(_gk, 13), (400000, 1), jnp.float32, 0.0, 1)
        return (x, src, dst, edge_attr_64, edge_weight1)
    x, src, dst, edge_attr_64, edge_weight1 = _rec_inputs()

    def _L0_gnn_setup():
        import jax, jax.numpy as jnp
        import numpy as np
        N_NODES = 12500
        N_EDGES = 800000
        H = 16
        RF_DIM = 64
        key = jax.random.key(seed)
        ks = jax.random.split(key, 7)
        feat = jax.random.normal(ks[0], (N_NODES, H), dtype=jnp.float32)
        review_feat = jax.random.normal(ks[1], (N_EDGES, RF_DIM), dtype=jnp.float32)
        edge_w = jax.random.uniform(ks[2], (N_EDGES, 1), dtype=jnp.float32)
        src_idx = jax.random.randint(ks[3], (N_EDGES,), 0, N_NODES, dtype=jnp.int32)
        dst_idx = jax.random.randint(ks[4], (N_EDGES,), 0, N_NODES, dtype=jnp.int32)
        b1 = float(np.sqrt(6.0 / (H + H)))
        W_node = jax.random.uniform(ks[5], (H, H), minval=-b1, maxval=b1, dtype=jnp.float32)
        b2 = float(np.sqrt(6.0 / (H + RF_DIM)))
        W_review = jax.random.uniform(ks[6], (H, RF_DIM), minval=-b2, maxval=b2, dtype=jnp.float32)
        return {'feat': feat, 'review_feat': review_feat, 'edge_w': edge_w, 'src_idx': src_idx, 'dst_idx': dst_idx, 'W_node': W_node, 'W_review': W_review}
    _L0_gnn_all = _L0_gnn_setup()
    _L0_gnn_in = {k: v for k, v in _L0_gnn_all.items() if k in ('W_node', 'W_review')}
    del _L0_gnn_all
    return {'x': x, 'src': src, 'dst': dst, 'edge_attr_64': edge_attr_64, 'edge_weight1': edge_weight1, 'L0_gnn_W_node': _L0_gnn_in['W_node'], 'L0_gnn_W_review': _L0_gnn_in['W_review']}

def reference(x, src, dst, edge_attr_64, edge_weight1, L0_gnn_W_node, L0_gnn_W_review):
    import jax
    import jax.numpy as jnp

    def _L0_gnn_ref(feat, review_feat, edge_w, src_idx, dst_idx, W_node, W_review):
        import jax, jax.numpy as jnp
        import numpy as np
        N_NODES = 12500
        N_EDGES = 800000
        H = 16
        RF_DIM = 64
        h = feat @ W_node.T
        rf = review_feat @ W_review.T
        m = (h[src_idx] + rf) * edge_w
        rst = jax.ops.segment_sum(m, dst_idx, num_segments=N_NODES)
        return rst
    h = jnp.maximum(_layernorm(x, axis=-1), 0.0)
    x = x + _L0_gnn_ref(h, edge_attr_64, edge_weight1, src, dst, L0_gnn_W_node, L0_gnn_W_review)
    return x

_drawn_inputs = setup_inputs


def setup_inputs(seed=0):
    import zlib

    import numpy as np

    out = dict(_drawn_inputs(seed))
    spreads = {}
    factors = {}
    for name, (base, spread) in spreads.items():
        noise = np.random.default_rng([zlib.crc32(name.encode()), seed]).standard_normal(out[name].shape)
        drawn = base * np.exp(spread * noise) if base else spread * noise
        out[name] = jnp.asarray(drawn.astype(out[name].dtype))
    for name, factor in factors.items():
        out[name] = (out[name] * factor).astype(out[name].dtype)
    return out
```

```python
from contextlib import ExitStack

import concourse.bass as bass
from concourse import mybir

ALU = mybir.AluOpType
ACT = mybir.ActivationFunctionType
AX = mybir.AxisListType
F32 = mybir.dt.float32
I32 = mybir.dt.int32

P = 128
J = 5
S = 5
T = S * J
GROUP = J * P
CHUNK = S * GROUP
WINDOW = 64
EPS = 1e-5


def bass_gnn_preln(
    nc: bass.Bass,
    x: bass.AP,
    src: bass.AP,
    dst: bass.AP,
    edge_attr: bass.AP,
    edge_weight: bass.AP,
    w_node: bass.AP,
    w_review: bass.AP,
    out: bass.AP,
):
    N, H = x.shape
    E, R = edge_attr.shape
    F = R + H
    C = E // CHUNK
    NP = N // C
    assert E == C * CHUNK and C <= P and N == C * NP and F <= P

    h_table = nc.dram_tensor("h_table", (N, H), F32, kind="Internal").ap()
    base_dram = nc.dram_tensor("base_dram", (2, C * S), F32, kind="Internal").ap()

    BANK = 512
    QUAD = 4
    parts = [(k, min(QUAD, T - k)) for k in range(0, T, QUAD)]
    NB = BANK // H
    out_parts = [(i, min(NB, NP - i)) for i in range(0, NP, NB)]

    with ExitStack() as ctx:
        def sb(name, shape, dt=F32):
            return ctx.enter_context(nc.sbuf_tensor(name, shape, dt))

        def sem(name):
            return ctx.enter_context(nc.semaphore(name))

        x_sb = sb("x_sb", [C, NP, H])
        xc = sb("xc", [C, NP, H])
        sq = sb("sq", [C, NP, H])
        stat = sb("stat", [C, 4, NP])
        ident = sb("ident", [P, P])
        iota_i = sb("iota_i", [P, WINDOW], I32)
        iota = sb("iota", [P, WINDOW])
        w_rows = sb("w_rows", [H, F])
        w_cols = sb("w_cols", [F, H])
        src_i = sb("src_i", [C, CHUNK], I32)
        dst_i = sb("dst_i", [C, CHUNK], I32)
        src_f = sb("src_f", [C, CHUNK])
        dst_f = sb("dst_f", [C, CHUNK])
        wgt_f = sb("wgt_f", [C, CHUNK])
        span = sb("span", [C, 3, S])
        span_row = sb("span_row", [1, 2, C * S])
        reach = sb("reach", [1, 1])
        reach_i = sb("reach_i", [1, 1], I32)
        base_row = sb("base_row", [1, C * S], I32)
        src_t = sb("src_t", [P, C, T], I32)
        rel_t = sb("rel_t", [P, C, T])
        wgt_t = sb("wgt_t", [P, C, T])
        idx = sb("idx", [P, S, J], I32)
        vals = sb("vals", [P, S, J, F])
        sel = sb("sel", [P, S, J, WINDOW])
        acc = sb("acc", [F, N + WINDOW])
        out_sb = sb("out_sb", [C, NP * H])
        banks = [ctx.enter_context(nc.psum_tensor(f"bank{i}", [P, BANK], F32)) for i in range(8)]
        seg = banks[:S]
        turn = banks[S:]

        x_in = sem("x_in")
        src_in = sem("src_in")
        dst_in = sem("dst_in")
        wgt_in = sem("wgt_in")
        w_in = sem("w_in")
        ident_zero = sem("ident_zero")
        ident_done = sem("ident_done")
        iota_made = sem("iota_made")
        chain = sem("chain")
        var_done = sem("var_done")
        std_done = sem("std_done")
        h_done = sem("h_done")
        h_stored = sem("h_stored")
        src_float = sem("src_float")
        rel_done = sem("rel_done")
        span_done = sem("span_done")
        span_out = sem("span_out")
        span_in = sem("span_in")
        reach_done = sem("reach_done")
        turned = sem("turned")
        src_placed = sem("src_placed")
        rel_placed = sem("rel_placed")
        wgt_placed = sem("wgt_placed")
        w_turned = sem("w_turned")
        w_placed = sem("w_placed")
        ea_in = [sem(f"ea_in{s}") for s in range(S)]
        idx_in = [sem(f"idx_in{s}") for s in range(S)]
        h_in = [sem(f"h_in{s}") for s in range(S)]
        sel_in = [sem(f"sel_in{s}") for s in range(S)]
        slot_free = [sem(f"slot_free{s}") for s in range(S)]
        slots_begun = sem("slots_begun")
        acc_step = sem("acc_step")
        shifted = sem("shifted")
        all_added = sem("all_added")
        product = sem("product")
        out_done = sem("out_done")
        out_stored = sem("out_stored")


        block = ctx.enter_context(nc.Block())

        def passes_on(eng):
            eng.wait_ge(reach_done, 1)
            far = eng.value_load(reach_i[0:1, 0:1], min_val=0, max_val=N)
            return far // WINDOW + 1

        @block.sync
        def _(sp):
            sp.dma_start(src_i[:], src.rearrange("(c e) -> c e", c=C)).then_inc(src_in, 16)
            sp.dma_start(x_sb[:], x.rearrange("(p i) f -> p i f", p=C)).then_inc(x_in, 16)
            sp.dma_start(dst_i[:], dst.rearrange("(c e) -> c e", c=C)).then_inc(dst_in, 16)
            sp.dma_start(wgt_f[:], edge_weight.rearrange("(c e) o -> c (e o)", c=C)).then_inc(wgt_in, 16)
            sp.dma_start(w_rows[:, 0:R], w_review).then_inc(w_in, 16)
            sp.dma_start(w_rows[:, R:F], w_node).then_inc(w_in, 16)
            sp.wait_ge(h_done, 1)
            sp.dma_start(h_table.rearrange("(p i) f -> p i f", p=C), xc[:]).then_inc(h_stored, 16)
            sp.wait_ge(span_done, 1)
            sp.dma_start(base_dram.rearrange("k (c s) -> c k s", c=C), span[:, 0:2, :]).then_inc(span_out, 16)
            sp.wait_ge(span_out, 16)
            sp.dma_start(span_row[:], base_dram.rearrange("(o k) g -> o k g", o=1)).then_inc(span_in, 16)
            with sp.Fori(0, passes_on(sp)) as ps:
                with sp.Fori(0, C) as c:
                    turn_no = sp.snap(ps * C + c + 1)
                    for s in range(S):
                        sp.wait_ge(slot_free[s], turn_no)
                        rows = edge_attr[bass.ds(c * CHUNK + s * GROUP, GROUP), :]
                        sp.dma_start(vals[:, s, :, 0:R], rows.rearrange("(p j) f -> p j f", j=J)).then_inc(ea_in[s], 16)
            for n, (i, k) in enumerate(out_parts):
                sp.wait_ge(out_done, n + 1)
                sp.dma_start(out.rearrange("(p i) f -> p (i f)", p=C)[:, i * H:(i + k) * H],
                             out_sb[:, i * H:(i + k) * H]).then_inc(out_stored, 16)
            sp.wait_ge(out_stored, 16 * len(out_parts))

        @block.gpsimd
        def _(pool):
            nc.gpsimd.memset(ident[:], 0.0).then_inc(ident_zero, 1)
            pool.wait_ge(ident_zero, 1)
            nc.gpsimd.affine_select(out=ident[:], in_=ident[:], compare_op=ALU.not_equal, fill=1.0, base=0,
                                    pattern=[[-1, P]], channel_multiplier=1).then_inc(ident_done, 1)
            nc.gpsimd.iota(iota_i[:], pattern=[[1, WINDOW]], base=0, channel_multiplier=0).then_inc(iota_made, 1)
            nc.gpsimd.memset(acc[:], 0.0).then_inc(acc_step, 1)
            loops = passes_on(pool)
            pool.wait_ge(h_stored, 16)
            with pool.Fori(0, loops) as ps:
                with pool.Fori(0, C) as c:
                    turn_no = pool.snap(ps * C + c + 1)
                    for s in range(S):
                        pool.wait_ge(idx_in[s], turn_no)
                        pool.sem_inc(slots_begun, 1)
                        for j in range(J):
                            pool.indirect_dma_start(
                                vals[:, s, j, R:F], None, h_table,
                                bass.IndirectOffsetOnAxis(ap=idx[:, s, j:j + 1], axis=0),
                            ).then_inc(h_in[s], 16)

        @block.scalar
        def _(act):
            act.wait_ge(src_in, 16)
            nc.scalar.copy(src_f[:], src_i[:]).then_inc(src_float, 1)
            act.wait_ge(var_done, 1)
            nc.scalar.activation(stat[:, 2, :], stat[:, 1, :], ACT.Sqrt).then_inc(std_done, 1)
            for n, (k, m) in enumerate(parts):
                act.wait_ge(turned, n + 1)
                nc.scalar.copy(src_t[:, :, k:k + m].rearrange("p c k -> p k c"),
                               turn[n % 3][:, 0:m * C].rearrange("p (k c) -> p k c", c=C)).then_inc(src_placed, 1)
            loops = passes_on(act)
            act.wait_ge(src_placed, len(parts))
            with act.Fori(0, loops) as ps:
                with act.Fori(0, C) as c:
                    turn_no = act.snap(ps * C + c + 1)
                    for s in range(S):
                        act.wait_ge(slot_free[s], turn_no)
                        nc.scalar.copy(idx[:, s, :], src_t[:, bass.ds(c, 1), s * J:(s + 1) * J].rearrange("p o j -> p (o j)")
                                       ).then_inc(idx_in[s], 1)

        @block.vector
        def _(dve):
            steps = [0]

            def link(ins):
                steps[0] += 1
                ins.then_inc(chain, 1)
                dve.wait_ge(chain, steps[0])

            dve.wait_ge(x_in, 16)
            link(nc.vector.tensor_reduce(stat[:, 0, :], x_sb[:], AX.X, ALU.add))
            link(nc.vector.tensor_scalar(stat[:, 1, :], stat[:, 0, :], 1.0 / H, None, ALU.mult))
            link(nc.vector.tensor_tensor(xc[:], x_sb[:], stat[:, 1, :].unsqueeze(2).to_broadcast([C, NP, H]), ALU.subtract))
            link(nc.vector.tensor_tensor(sq[:], xc[:], xc[:], ALU.mult))
            link(nc.vector.tensor_reduce(stat[:, 0, :], sq[:], AX.X, ALU.add))
            nc.vector.tensor_scalar(stat[:, 1, :], stat[:, 0, :], 1.0 / H, EPS, ALU.mult, ALU.add).then_inc(var_done, 1)
            dve.wait_ge(std_done, 1)
            link(nc.vector.reciprocal(stat[:, 3, :], stat[:, 2, :]))
            nc.vector.scalar_tensor_tensor(out=xc[:], in0=xc[:], scalar=0.0,
                                           in1=stat[:, 3, :].unsqueeze(2).to_broadcast([C, NP, H]),
                                           op0=ALU.max, op1=ALU.mult).then_inc(h_done, 1)
            dve.wait_ge(dst_in, 16)
            link(nc.vector.tensor_scalar(dst_f[:], dst_i[:], float(N), None, ALU.min))
            by_group = dst_f[:].rearrange("c (s e) -> c s e", s=S)
            link(nc.vector.tensor_reduce(span[:, 0, :], by_group, AX.X, ALU.min))
            link(nc.vector.tensor_reduce(span[:, 2, :], by_group, AX.X, ALU.max))
            nc.vector.tensor_tensor(span[:, 1, :], span[:, 2, :], span[:, 0, :], ALU.subtract).then_inc(span_done, 1)
            nc.vector.tensor_tensor(by_group, by_group, span[:, 0, :].unsqueeze(2).to_broadcast([C, S, GROUP]),
                                    ALU.subtract).then_inc(rel_done, 1)
            dve.wait_ge(iota_made, 1)
            link(nc.vector.tensor_copy(iota[:], iota_i[:]))
            for a, (placed, dest) in enumerate(((rel_placed, rel_t), (wgt_placed, wgt_t))):
                for i, (k, m) in enumerate(parts):
                    n = (a + 1) * len(parts) + i
                    dve.wait_ge(turned, n + 1)
                    nc.vector.tensor_copy(dest[:, :, k:k + m].rearrange("p c k -> p k c"),
                                          turn[n % 3][:, 0:m * C].rearrange("p (k c) -> p k c", c=C)).then_inc(placed, 1)
            dve.wait_ge(w_turned, 1)
            nc.vector.tensor_copy(w_cols[:], turn[0][0:F, 0:H]).then_inc(w_placed, 1)
            dve.wait_ge(span_in, 16)
            link(nc.vector.tensor_copy(base_row[:], span_row[:, 0, :]))
            link(nc.vector.tensor_reduce(reach[:], span_row[:, 1, :], AX.X, ALU.max))
            nc.vector.tensor_copy(reach_i[:], reach[:]).then_inc(reach_done, 1)
            loops = passes_on(dve)
            dve.wait_ge(rel_placed, len(parts))
            dve.wait_ge(wgt_placed, len(parts))
            with dve.Fori(0, loops) as ps:
                with dve.Fori(0, C) as c:
                    turn_no = dve.snap(ps * C + c + 1)
                    step = dve.snap((ps * C + c) * S + 1)
                    dve.wait_ge(acc_step, step)
                    for s in range(S):
                        dve.wait_ge(slot_free[s], turn_no)
                        for j in range(J):
                            k = s * J + j
                            made = nc.vector.tensor_scalar(sel[:, s, j, :], iota[:],
                                                           rel_t[:, bass.ds(c, 1), k:k + 1].rearrange("p o k -> p (o k)"),
                                                           wgt_t[:, bass.ds(c, 1), k:k + 1].rearrange("p o k -> p (o k)"),
                                                           ALU.is_equal, ALU.mult)
                        made.then_inc(sel_in[s], 1)
                    for s in range(S):
                        base = dve.value_load(base_row[0:1, bass.ds(c * S + s, 1)], min_val=0, max_val=N)
                        dve.wait_ge(slot_free[s], turn_no + 1)
                        dve.wait_ge(acc_step, step + s)
                        window = acc[:, bass.ds(base, WINDOW)]
                        nc.vector.tensor_tensor(window, window, seg[s][0:F, 0:WINDOW], ALU.add).then_inc(acc_step, 1)
                nc.vector.tensor_scalar(rel_t[:], rel_t[:], float(WINDOW), None, ALU.subtract).then_inc(shifted, 1)
                nc.vector.tensor_scalar(base_row[:], base_row[:], float(WINDOW), float(N), ALU.add, ALU.min).then_inc(shifted, 1)
                dve.wait_ge(shifted, ps * 2 + 2)
            dve.wait_ge(acc_step, loops * (C * S) + 1)
            nc.vector.tensor_copy(reach[:], reach_i[:]).then_inc(all_added, 1)
            for n, (i, k) in enumerate(out_parts):
                dve.wait_ge(product, n + 1)
                nc.vector.tensor_tensor(out_sb[:, i * H:(i + k) * H], x_sb[:, i:i + k, :].rearrange("p i f -> p (i f)"),
                                        seg[n][0:C, 0:k * H], ALU.add).then_inc(out_done, 1)

        @block.tensor
        def _(pe):
            pe.wait_ge(ident_done, 1)
            for s in range(S):
                pe.sem_inc(slot_free[s], 1)
            n = 0
            for source, ready, count in ((src_f, src_float, 1), (dst_f, rel_done, 1), (wgt_f, wgt_in, 16)):
                pe.wait_ge(ready, count)
                tiles = source[:].rearrange("c (s p j) -> c s j p", s=S, j=J)
                for k, m in parts:
                    if n >= 3:
                        a, i = divmod(n - 3, len(parts))
                        pe.wait_ge((src_placed, rel_placed, wgt_placed)[a], i + 1)
                    for q in range(m):
                        s, j = divmod(k + q, J)
                        last = nc.tensor.transpose(turn[n % 3][:, q * C:(q + 1) * C], tiles[:, s, j, :], ident[0:C, 0:C])
                    last.then_inc(turned, 1)
                    n += 1
            pe.wait_ge(wgt_placed, len(parts))
            pe.wait_ge(w_in, 32)
            nc.tensor.transpose(turn[0][0:F, 0:H], w_rows[:], ident[0:H, 0:H]).then_inc(w_turned, 1)
            loops = passes_on(pe)
            with pe.Fori(0, loops) as ps:
                with pe.Fori(0, C) as c:
                    turn_no = pe.snap(ps * C + c + 1)
                    for s in range(S):
                        pe.wait_ge(sel_in[s], turn_no)
                        pe.wait_ge(ea_in[s], turn_no * 16)
                        pe.wait_ge(h_in[s], turn_no * (16 * J))
                        for j in range(J):
                            last = nc.tensor.matmul(seg[s][0:F, 0:WINDOW], vals[:, s, j, :], sel[:, s, j, :],
                                                    start=(j == 0), stop=(j == J - 1))
                        last.then_inc(slot_free[s], 1)
            pe.wait_ge(w_placed, 1)
            pe.wait_ge(all_added, 1)
            by_rest = acc[:, 0:N].rearrange("f (p i) -> f i p", i=NP)
            for n, (i, k) in enumerate(out_parts):
                for q in range(k):
                    last = nc.tensor.matmul(seg[n][0:C, q * H:(q + 1) * H], by_rest[:, i + q, :], w_cols[:],
                                            start=True, stop=True)
                last.then_inc(product, 1)


_INS = ["x", "src", "dst", "edge_attr_64", "edge_weight1", "L0_gnn_W_node", "L0_gnn_W_review"]
_OUTS = [((12500, 16), "float32")]


def kernel(**inputs):
    import numpy as _np
    import concourse.bacc as _bacc
    from concourse import mybir as _mybir
    from concourse.bass_utils import run_bass_kernel_spmd as _run

    nc = _bacc.Bacc("TRN2", target_bir_lowering=False, num_devices=1)
    arrays, args = {}, []
    for name in _INS:
        a = _np.ascontiguousarray(inputs[name])
        arrays[f"in_{name}_dram"] = a
        args.append(nc.dram_tensor(f"in_{name}_dram", a.shape, _mybir.dt.from_np(a.dtype), kind="ExternalInput").ap())
    for i, (shape, dtype) in enumerate(_OUTS):
        dt = _mybir.dt.from_np(_np.dtype(dtype))
        args.append(nc.dram_tensor(f"out_{i}_dram", shape, dt, kind="ExternalOutput").ap())
    bass_gnn_preln(nc, *args)
    r = _run(nc, [arrays], core_ids=[0])
    got = tuple(r.results[0][f"out_{i}_dram"] for i in range(len(_OUTS)))
    return got[0]
```

```python
from contextlib import ExitStack

import concourse.bass as bass
from concourse import mybir

ALU = mybir.AluOpType
ACT = mybir.ActivationFunctionType
AX = mybir.AxisListType
F32 = mybir.dt.float32
I32 = mybir.dt.int32
F16 = mybir.dt.float16

P = 128
J = 5
S = 5
T = S * J
GROUP = J * P
CHUNK = S * GROUP
WINDOW = 64
EPS = 1e-5

PE_TILES = (2, 3, 3, 2, 0)
HALVES = ((0, 1), (2, 3))
ORDER = (0, 1, 2, 4, 3)
G = sum(PE_TILES)
FIRST = [sum(PE_TILES[:s]) for s in range(S)]
NBD = 14
NA = 7
FOUND = 256
DIGIT_B = NA * P
SCALE = 8192.0


def bass_gnn_preln(
    nc: bass.Bass,
    x: bass.AP,
    src: bass.AP,
    dst: bass.AP,
    edge_attr: bass.AP,
    edge_weight: bass.AP,
    w_node: bass.AP,
    w_review: bass.AP,
    out: bass.AP,
):
    N, H = x.shape
    E, R = edge_attr.shape
    F = R + H
    C = E // CHUNK
    NP = N // C
    assert E == C * CHUNK and C <= P and N == C * NP and F <= P

    assert N <= NBD * DIGIT_B and DIGIT_B <= 2048 and NBD * H <= FOUND
    NPAD = NBD * DIGIT_B

    h_table = nc.dram_tensor("h_table", (NPAD, H), F32, kind="Internal").ap()
    low_dram = nc.dram_tensor("low_dram", (C, G * P), F16, kind="Internal").ap()
    base_dram = nc.dram_tensor("base_dram", (2, C * S), F32, kind="Internal").ap()

    BANK = 512
    QUAD = 4
    parts = [(k, min(QUAD, T - k)) for k in range(0, T, QUAD)]
    high_parts = [(k, min(QUAD, G - k)) for k in range(0, G, QUAD)]
    NB = BANK // H
    out_parts = [(i, min(NB, NP - i)) for i in range(0, NP, NB)]

    with ExitStack() as ctx:
        def sb(name, shape, dt=F32):
            return ctx.enter_context(nc.sbuf_tensor(name, shape, dt))

        def sem(name):
            return ctx.enter_context(nc.semaphore(name))

        x_sb = sb("x_sb", [C, NP, H])
        xc = sb("xc", [C, NP, H])
        work = sb("work", [P, NP * H])
        sq = work[0:C, :].rearrange("p (i f) -> p i f", f=H)
        h_rows = work[:, 0:NPAD // P * H]
        out_sb = work[0:C, :]
        stat = sb("stat", [C, 4, NP])
        ident = sb("ident", [P, P])
        iota_i = sb("iota_i", [P, WINDOW], I32)
        iota = sb("iota", [P, WINDOW])
        w_rows = sb("w_rows", [H, F])
        w_cols = sb("w_cols", [F, H])
        arena = sb("arena", [P, 3 * CHUNK])
        src_f = arena[0:C, 0:CHUNK]
        dst_f = arena[0:C, CHUNK:2 * CHUNK]
        wgt_f = arena[0:C, 2 * CHUNK:3 * CHUNK]
        src_i = src_f.bitcast(I32)
        dst_i = dst_f.bitcast(I32)
        hot = []
        at = 0
        for groups in HALVES:
            n = P * sum(PE_TILES[s] for s in groups)
            hot.append(arena[:, at:at + NA * n // 2].bitcast(F16).rearrange("p (a n) -> p a n", a=NA))
            at += NA * n // 2
        span = sb("span", [C, 3, S])
        span_row = sb("span_row", [1, 2, C * S])
        reach = sb("reach", [1, 1])
        reach_i = sb("reach_i", [1, 1], I32)
        base_row = sb("base_row", [1, C * S], I32)
        src_t = sb("src_t", [P, C, T], I32)
        rel_t = sb("rel_t", [P, C, T])
        wgt_t = sb("wgt_t", [P, C, T])
        idx = sb("idx", [P, S, J], I32)
        vals = sb("vals", [P, S, J, F])
        hit = sb("hit", [P, S, J, WINDOW], F16)
        sel = sb("sel", [P, S, J, WINDOW])
        pe_src = vals[0:C].rearrange("p s j f -> p (s j f)")[:, 0:G * P]
        pe_cut = sel[0:C].rearrange("p s j w -> p (s j w)")[:, 0:G * P]
        high = sb("high", [C, G * P])
        low = sb("low", [C, G * P], F16)
        low_all = sb("low_all", [P, G * P], F16)
        high_t = sb("high_t", [P, C, G])
        own_i = sb("own_i", [P, NA], I32)
        own = sb("own", [P, NA])
        digit_i = sb("digit_i", [P, NBD], I32)
        digit = sb("digit", [P, NBD])
        table = sb("table", [P, NA, 2, NBD * H], F16)
        zeros = sb("zeros", [P, H])
        pick = sb("pick", [P, G, NBD])
        picked_h = sb("picked_h", [P, 2, max(PE_TILES) * NBD * H])
        acc = sb("acc", [F, N + WINDOW])
        banks = [ctx.enter_context(nc.psum_tensor(f"bank{i}", [P, BANK], F32)) for i in range(4)]
        seg = [banks[0], banks[1], banks[2], banks[3], banks[0][:, BANK // 2:BANK]]
        found = [ctx.enter_context(nc.psum_tensor(f"found{i}", [P, 2 * BANK], F32)) for i in range(2)]
        turn = [found[0][:, 0:BANK], found[0][:, BANK:2 * BANK], found[1][:, 0:BANK]]

        x_in = sem("x_in")
        src_in = sem("src_in")
        zeros_made = sem("zeros_made")
        zeros_stored = sem("zeros_stored")
        h_back = sem("h_back")
        low_done = sem("low_done")
        high_done = sem("high_done")
        low_stored = sem("low_stored")
        high_placed = sem("high_placed")
        table_done = sem("table_done")
        src_read = sem("src_read")
        low_in = [sem("low_in_a"), sem("low_in_b")]
        hot_in = [sem("hot_in_a"), sem("hot_in_b")]
        found_in = [sem(f"found_in{s}") for s in range(S)]
        masked = [sem(f"masked{s}") for s in range(S)]
        pick_in = sem("pick_in")
        picked = [sem(f"picked{s}") for s in range(S)]
        hit_in = [sem(f"hit_in{s}") for s in range(S)]
        dst_in = sem("dst_in")
        wgt_in = sem("wgt_in")
        w_in = sem("w_in")
        ident_zero = sem("ident_zero")
        ident_done = sem("ident_done")
        iota_made = sem("iota_made")
        chain = sem("chain")
        var_done = sem("var_done")
        std_done = sem("std_done")
        h_done = sem("h_done")
        h_stored = sem("h_stored")
        src_float = sem("src_float")
        rel_done = sem("rel_done")
        span_done = sem("span_done")
        span_out = sem("span_out")
        span_in = sem("span_in")
        reach_done = sem("reach_done")
        turned = sem("turned")
        src_placed = sem("src_placed")
        rel_placed = sem("rel_placed")
        wgt_placed = sem("wgt_placed")
        w_turned = sem("w_turned")
        w_placed = sem("w_placed")
        ea_in = [sem(f"ea_in{s}") for s in range(S)]
        idx_in = [sem(f"idx_in{s}") for s in range(S)]
        h_in = [sem(f"h_in{s}") for s in range(S)]
        sel_in = [sem(f"sel_in{s}") for s in range(S)]
        slot_free = [sem(f"slot_free{s}") for s in range(S)]
        slots_begun = sem("slots_begun")
        acc_step = sem("acc_step")
        shifted = sem("shifted")
        all_added = sem("all_added")
        product = sem("product")
        out_done = sem("out_done")
        out_stored = sem("out_stored")


        block = ctx.enter_context(nc.Block())

        def columns(half):
            start = FIRST[HALVES[half][0]]
            return slice(P * start, P * (start + sum(PE_TILES[s] for s in HALVES[half])))

        def passes_on(eng):
            eng.wait_ge(reach_done, 1)
            far = eng.value_load(reach_i[0:1, 0:1], min_val=0, max_val=N)
            return far // WINDOW + 1

        @block.sync
        def _(sp):
            sp.dma_start(src_i, src.rearrange("(c e) -> c e", c=C)).then_inc(src_in, 16)
            sp.dma_start(x_sb[:], x.rearrange("(p i) f -> p i f", p=C)).then_inc(x_in, 16)
            sp.dma_start(dst_i, dst.rearrange("(c e) -> c e", c=C)).then_inc(dst_in, 16)
            sp.dma_start(wgt_f, edge_weight.rearrange("(c e) o -> c (e o)", c=C)).then_inc(wgt_in, 16)
            sp.dma_start(w_rows[:, 0:R], w_review).then_inc(w_in, 16)
            sp.dma_start(w_rows[:, R:F], w_node).then_inc(w_in, 16)
            sp.wait_ge(h_done, 1)
            sp.dma_start(h_table[0:N, :].rearrange("(p i) f -> p i f", p=C), xc[:]).then_inc(h_stored, 16)
            sp.wait_ge(zeros_made, 1)
            sp.dma_start(h_table[N:NPAD, :], zeros[0:NPAD - N, :]).then_inc(zeros_stored, 16)
            sp.wait_ge(h_stored, 16)
            sp.wait_ge(zeros_stored, 16)
            sp.dma_start(h_rows.rearrange("p (k f) -> p k f", f=H),
                         h_table.rearrange("(k p) f -> p k f", p=P)).then_inc(h_back, 16)
            sp.wait_ge(span_done, 1)
            sp.dma_start(base_dram.rearrange("k (c s) -> c k s", c=C), span[:, 0:2, :]).then_inc(span_out, 16)
            sp.wait_ge(span_out, 16)
            sp.dma_start(span_row[:], base_dram.rearrange("(o k) g -> o k g", o=1)).then_inc(span_in, 16)
            sp.wait_ge(low_done, 1)
            sp.dma_start(low_dram, low[:]).then_inc(low_stored, 16)
            sp.wait_ge(low_stored, 16)

            def load_low(half, chunk):
                cols = columns(half)
                sp.dma_start(low_all[:, cols], low_dram[bass.ds(chunk, 1), cols].to_broadcast([P, cols.stop - cols.start])
                             ).then_inc(low_in[half], 16)

            load_low(0, 0)
            load_low(1, 0)
            loops = passes_on(sp)
            with sp.Fori(0, loops) as ps:
                with sp.Fori(0, C) as c:
                    turn_no = sp.snap(ps * C + c + 1)
                    for s in ORDER:
                        sp.wait_ge(slot_free[s], turn_no)
                        rows = edge_attr[bass.ds(c * CHUNK + s * GROUP, GROUP), :]
                        sp.dma_start(vals[:, s, :, 0:R], rows.rearrange("(p j) f -> p j f", j=J)).then_inc(ea_in[s], 16)
                    next_chunk = sp.snap((c + 1) % C)
                    for half in range(2):
                        sp.wait_ge(hot_in[half], turn_no)
                        load_low(half, next_chunk)
            for half in range(2):
                sp.wait_ge(low_in[half], loops * (C * 16) + 16)
            for n, (i, k) in enumerate(out_parts):
                sp.wait_ge(out_done, n + 1)
                sp.dma_start(out.rearrange("(p i) f -> p (i f)", p=C)[:, i * H:(i + k) * H],
                             out_sb[:, i * H:(i + k) * H]).then_inc(out_stored, 16)
            sp.wait_ge(out_stored, 16 * len(out_parts))

        @block.gpsimd
        def _(pool):
            nc.gpsimd.memset(ident[:], 0.0).then_inc(ident_zero, 1)
            pool.wait_ge(ident_zero, 1)
            nc.gpsimd.affine_select(out=ident[:], in_=ident[:], compare_op=ALU.not_equal, fill=1.0, base=0,
                                    pattern=[[-1, P]], channel_multiplier=1).then_inc(ident_done, 1)
            nc.gpsimd.iota(iota_i[:], pattern=[[1, WINDOW]], base=0, channel_multiplier=0).then_inc(iota_made, 1)
            nc.gpsimd.iota(own_i[:], pattern=[[P, NA]], base=0, channel_multiplier=1).then_inc(iota_made, 1)
            nc.gpsimd.iota(digit_i[:], pattern=[[DIGIT_B, NBD]], base=0, channel_multiplier=0).then_inc(iota_made, 1)
            nc.gpsimd.memset(zeros[:], 0.0).then_inc(zeros_made, 1)
            nc.gpsimd.memset(acc[:], 0.0).then_inc(acc_step, 1)
            loops = passes_on(pool)
            pool.wait_ge(h_stored, 16)
            with pool.Fori(0, loops) as ps:
                with pool.Fori(0, C) as c:
                    turn_no = pool.snap(ps * C + c + 1)
                    for s in ORDER:
                        pool.wait_ge(idx_in[s], turn_no)
                        pool.sem_inc(slots_begun, 1)
                        for j in range(J - PE_TILES[s]):
                            pool.indirect_dma_start(
                                vals[:, s, j, R:F], None, h_table,
                                bass.IndirectOffsetOnAxis(ap=idx[:, s, j:j + 1], axis=0),
                            ).then_inc(h_in[s], 16)

        @block.scalar
        def _(act):
            act.wait_ge(src_in, 16)
            nc.scalar.copy(src_f, src_i).then_inc(src_float, 1)
            act.wait_ge(var_done, 1)
            nc.scalar.activation(stat[:, 2, :], stat[:, 1, :], ACT.Sqrt).then_inc(std_done, 1)
            for n, (k, m) in enumerate(parts):
                act.wait_ge(turned, n + 1)
                nc.scalar.copy(src_t[:, :, k:k + m].rearrange("p c k -> p k c"),
                               turn[n % 3][:, 0:m * C].rearrange("p (k c) -> p k c", c=C)).then_inc(src_placed, 1)
            loops = passes_on(act)
            act.wait_ge(src_placed, len(parts))
            act.wait_ge(wgt_placed, len(parts))
            with act.Fori(0, loops) as ps:
                with act.Fori(0, C) as c:
                    turn_no = act.snap(ps * C + c + 1)
                    for s in ORDER:
                        act.wait_ge(slot_free[s], turn_no)
                        nc.scalar.copy(idx[:, s, :], src_t[:, bass.ds(c, 1), s * J:(s + 1) * J].rearrange("p o j -> p (o j)")
                                       ).then_inc(idx_in[s], 1)
                    for s in ORDER:
                        act.wait_ge(hit_in[s], turn_no)
                        for j in range(J):
                            k = s * J + j
                            made = nc.scalar.activation(sel[:, s, j, :], hit[:, s, j, :], ACT.Copy,
                                                        scale=wgt_t[:, bass.ds(c, 1), k:k + 1].rearrange("p o k -> p (o k)"))
                        made.then_inc(sel_in[s], 1)

        @block.vector
        def _(dve):
            steps = [0]

            def link(ins):
                steps[0] += 1
                ins.then_inc(chain, 1)
                dve.wait_ge(chain, steps[0])

            dve.wait_ge(x_in, 16)
            link(nc.vector.tensor_reduce(stat[:, 0, :], x_sb[:], AX.X, ALU.add))
            link(nc.vector.tensor_scalar(stat[:, 1, :], stat[:, 0, :], 1.0 / H, None, ALU.mult))
            link(nc.vector.tensor_tensor(xc[:], x_sb[:], stat[:, 1, :].unsqueeze(2).to_broadcast([C, NP, H]), ALU.subtract))
            link(nc.vector.tensor_tensor(sq[:], xc[:], xc[:], ALU.mult))
            link(nc.vector.tensor_reduce(stat[:, 0, :], sq[:], AX.X, ALU.add))
            nc.vector.tensor_scalar(stat[:, 1, :], stat[:, 0, :], 1.0 / H, EPS, ALU.mult, ALU.add).then_inc(var_done, 1)
            dve.wait_ge(std_done, 1)
            link(nc.vector.reciprocal(stat[:, 3, :], stat[:, 2, :]))
            nc.vector.scalar_tensor_tensor(out=xc[:], in0=xc[:], scalar=0.0,
                                           in1=stat[:, 3, :].unsqueeze(2).to_broadcast([C, NP, H]),
                                           op0=ALU.max, op1=ALU.mult).then_inc(h_done, 1)
            dve.wait_ge(dst_in, 16)
            link(nc.vector.tensor_scalar(dst_f, dst_i, float(N), None, ALU.min))
            by_group = dst_f.rearrange("c (s e) -> c s e", s=S)
            link(nc.vector.tensor_reduce(span[:, 0, :], by_group, AX.X, ALU.min))
            link(nc.vector.tensor_reduce(span[:, 2, :], by_group, AX.X, ALU.max))
            nc.vector.tensor_tensor(span[:, 1, :], span[:, 2, :], span[:, 0, :], ALU.subtract).then_inc(span_done, 1)
            nc.vector.tensor_tensor(by_group, by_group, span[:, 0, :].unsqueeze(2).to_broadcast([C, S, GROUP]),
                                    ALU.subtract).then_inc(rel_done, 1)
            dve.wait_ge(iota_made, 1)
            link(nc.vector.tensor_copy(iota[:], iota_i[:]))
            dve.wait_ge(src_float, 1)
            tiles = src_f.rearrange("c (s p j) -> c s j p", s=S, j=J)
            for s in range(S):
                if PE_TILES[s]:
                    last = nc.vector.tensor_copy(
                        pe_src[:, FIRST[s] * P:(FIRST[s] + PE_TILES[s]) * P].rearrange("c (g p) -> c g p", p=P),
                        tiles[:, s, J - PE_TILES[s]:J, :])
            last.then_inc(src_read, 1)
            dve.wait_ge(src_read, 1)
            rest = pe_src
            for bit in (8, 4, 2, 1):
                link(nc.vector.tensor_scalar(pe_cut, rest, float(bit * DIGIT_B), float(-bit * DIGIT_B), ALU.is_ge, ALU.mult))
                link(nc.vector.tensor_tensor(high[:], rest, pe_cut, ALU.add))
                rest = high[:]
            nc.vector.tensor_copy(low[:], high[:]).then_inc(low_done, 1)
            nc.vector.tensor_tensor(high[:], pe_src, high[:], ALU.subtract).then_inc(high_done, 1)
            dve.wait_ge(iota_made, 3)
            link(nc.vector.tensor_copy(own[:], own_i[:]))
            link(nc.vector.tensor_copy(digit[:], digit_i[:]))
            dve.wait_ge(h_back, 16)
            by_digit = h_rows.rearrange("p (b a f) -> p a b f", b=NBD, a=NA)
            parts_of = [table[:, :, i, :].rearrange("p a (b f) -> p a b f", f=H) for i in range(2)]
            for a in range(NA):
                last = nc.vector.tensor_scalar(parts_of[0][:, a], by_digit[:, a], SCALE, None, ALU.mult)
            link(last)
            for a in range(NA):
                last = nc.vector.scalar_tensor_tensor(out=parts_of[1][:, a], in0=by_digit[:, a], scalar=SCALE,
                                                      in1=parts_of[0][:, a], op0=ALU.mult, op1=ALU.subtract)
            last.then_inc(table_done, 1)
            for a, (placed, dest) in enumerate(((rel_placed, rel_t), (wgt_placed, wgt_t))):
                for i, (k, m) in enumerate(parts):
                    n = (a + 1) * len(parts) + i
                    dve.wait_ge(turned, n + 1)
                    nc.vector.tensor_copy(dest[:, :, k:k + m].rearrange("p c k -> p k c"),
                                          turn[n % 3][:, 0:m * C].rearrange("p (k c) -> p k c", c=C)).then_inc(placed, 1)
            for i, (k, m) in enumerate(high_parts):
                n = 3 * len(parts) + i
                dve.wait_ge(turned, n + 1)
                nc.vector.tensor_copy(high_t[:, :, k:k + m].rearrange("p c k -> p k c"),
                                      turn[n % 3][:, 0:m * C].rearrange("p (k c) -> p k c", c=C)).then_inc(high_placed, 1)
            dve.wait_ge(w_turned, 1)
            nc.vector.tensor_copy(w_cols[:], turn[0][0:F, 0:H]).then_inc(w_placed, 1)
            dve.wait_ge(span_in, 16)
            link(nc.vector.tensor_copy(base_row[:], span_row[:, 0, :]))
            link(nc.vector.tensor_reduce(reach[:], span_row[:, 1, :], AX.X, ALU.max))
            nc.vector.tensor_copy(reach_i[:], reach[:]).then_inc(reach_done, 1)
            loops = passes_on(dve)
            dve.wait_ge(rel_placed, len(parts))
            dve.wait_ge(wgt_placed, len(parts))
            dve.wait_ge(high_placed, len(high_parts))

            def make_hot(half):
                for a in range(NA):
                    made = nc.vector.tensor_scalar(hot[half][:, a, :], low_all[:, columns(half)], own[:, a:a + 1],
                                                   None, ALU.is_equal)
                made.then_inc(hot_in[half], 1)

            dve.wait_ge(turned, 3 * len(parts) + len(high_parts))
            dve.wait_ge(low_in[0], 16)
            make_hot(0)
            with dve.Fori(0, loops) as ps:
                with dve.Fori(0, C) as c:
                    turn_no = dve.snap(ps * C + c + 1)
                    step = dve.snap((ps * C + c) * S + 1)
                    dve.wait_ge(acc_step, step)
                    nc.vector.tensor_tensor(pick[:], high_t[:, bass.ds(c, 1), :].rearrange("p o g -> p (o g)").unsqueeze(2).to_broadcast([P, G, NBD]),
                                            digit[:].unsqueeze(1).to_broadcast([P, G, NBD]), ALU.is_equal).then_inc(pick_in, 1)
                    for s in ORDER:
                        dve.wait_ge(slot_free[s], turn_no)
                        nc.vector.tensor_tensor(hit[:, s], iota[:].unsqueeze(1).to_broadcast([P, J, WINDOW]),
                                                rel_t[:, bass.ds(c, 1), s * J:(s + 1) * J].rearrange("p o j -> p (o j)").unsqueeze(2).to_broadcast([P, J, WINDOW]),
                                                ALU.is_equal).then_inc(hit_in[s], 1)

                    def choose(s):
                        m = PE_TILES[s]
                        dve.wait_ge(found_in[s], turn_no)
                        dve.wait_ge(pick_in, turn_no)
                        if s >= 2:
                            dve.wait_ge(picked[s - 2], turn_no)
                        nc.vector.scalar_tensor_tensor(
                            out=picked_h[:, s % 2, 0:m * NBD * H].rearrange("p (g b f) -> p g b f", g=m, b=NBD),
                            in0=found[s % 2][:].rearrange("p (g n) -> p g n", n=FOUND)[:, 0:m, 0:NBD * H].rearrange("p g (b f) -> p g b f", b=NBD),
                            scalar=1.0 / SCALE,
                            in1=pick[:, FIRST[s]:FIRST[s] + m, :].unsqueeze(3).to_broadcast([P, m, NBD, H]),
                            op0=ALU.mult, op1=ALU.mult).then_inc(masked[s], 1)
                        dve.wait_ge(masked[s], turn_no)
                        nc.vector.tensor_reduce(vals[:, s, J - m:J, R:F],
                                                picked_h[:, s % 2, 0:m * NBD * H].rearrange("p (g b f) -> p g f b", g=m, b=NBD),
                                                AX.X, ALU.add).then_inc(picked[s], 1)

                    def add_up(n):
                        s = ORDER[n]
                        base = dve.value_load(base_row[0:1, bass.ds(c * S + s, 1)], min_val=0, max_val=N)
                        dve.wait_ge(slot_free[s], turn_no + 1)
                        dve.wait_ge(acc_step, step + n)
                        window = acc[:, bass.ds(base, WINDOW)]
                        nc.vector.tensor_tensor(window, window, seg[s][0:F, 0:WINDOW], ALU.add).then_inc(acc_step, 1)

                    choose(0)
                    dve.wait_ge(low_in[1], turn_no * 16)
                    make_hot(1)
                    choose(1)
                    add_up(0)
                    dve.wait_ge(low_in[0], turn_no * 16 + 16)
                    make_hot(0)
                    choose(2)
                    add_up(1)
                    choose(3)
                    add_up(2)
                    add_up(3)
                    add_up(4)
                nc.vector.tensor_scalar(rel_t[:], rel_t[:], float(WINDOW), None, ALU.subtract).then_inc(shifted, 1)
                nc.vector.tensor_scalar(base_row[:], base_row[:], float(WINDOW), float(N), ALU.add, ALU.min).then_inc(shifted, 1)
                dve.wait_ge(shifted, ps * 2 + 2)
            dve.wait_ge(acc_step, loops * (C * S) + 1)
            nc.vector.tensor_copy(reach[:], reach_i[:]).then_inc(all_added, 1)
            for n, (i, k) in enumerate(out_parts):
                dve.wait_ge(product, n + 1)
                nc.vector.tensor_tensor(out_sb[:, i * H:(i + k) * H], x_sb[:, i:i + k, :].rearrange("p i f -> p (i f)"),
                                        seg[n][0:C, 0:k * H], ALU.add).then_inc(out_done, 1)

        @block.tensor
        def _(pe):
            pe.wait_ge(ident_done, 1)
            for s in range(S):
                pe.sem_inc(slot_free[s], 1)
            n = 0
            by_tile = [a.rearrange("c (s p j) -> c s j p", s=S, j=J) for a in (src_f, dst_f, wgt_f)]
            by_tile = [[a[:, k // J, k % J, :] for k in range(T)] for a in by_tile]
            by_tile.append([high[:, g * P:(g + 1) * P] for g in range(G)])
            for tiles, ready, count in zip(by_tile, (src_float, rel_done, wgt_in, high_done), (1, 1, 16, 1)):
                pe.wait_ge(ready, count)
                for k, m in (parts if len(tiles) == T else high_parts):
                    if n >= 3:
                        a, i = divmod(n - 3, len(parts))
                        pe.wait_ge((src_placed, rel_placed, wgt_placed)[a], i + 1)
                    for q in range(m):
                        last = nc.tensor.transpose(turn[n % 3][:, q * C:(q + 1) * C], tiles[k + q], ident[0:C, 0:C])
                    last.then_inc(turned, 1)
                    n += 1
            pe.wait_ge(high_placed, len(high_parts))
            pe.wait_ge(w_in, 32)
            nc.tensor.transpose(turn[0][0:F, 0:H], w_rows[:], ident[0:H, 0:H]).then_inc(w_turned, 1)
            loops = passes_on(pe)
            pe.wait_ge(table_done, 1)
            pe.wait_ge(w_placed, 1)
            with pe.Fori(0, loops) as ps:
                with pe.Fori(0, C) as c:
                    turn_no = pe.snap(ps * C + c + 1)

                    def look_up(s):
                        half = s // 2
                        if s == HALVES[half][0]:
                            pe.wait_ge(hot_in[half], turn_no)
                        for a in range(NA):
                            for g in range(PE_TILES[s]):
                                at = (FIRST[s] + g) * P - columns(half).start
                                for part in range(2):
                                    last = nc.tensor.matmul(found[s % 2][:, g * FOUND:g * FOUND + NBD * H],
                                                            hot[half][:, a, at:at + P], table[:, a, part, :],
                                                            start=(a == 0 and g % 2 == 0 and part == 0),
                                                            stop=(a == NA - 1 and part == 1), skip_group_check=True)
                        last.then_inc(found_in[s], 1)

                    def sum_up(s):
                        pe.wait_ge(sel_in[s], turn_no)
                        pe.wait_ge(ea_in[s], turn_no * 16)
                        pe.wait_ge(h_in[s], turn_no * (16 * (J - PE_TILES[s])))
                        if PE_TILES[s]:
                            pe.wait_ge(picked[s], turn_no)
                        for j in range(J):
                            last = nc.tensor.matmul(seg[s][0:F, 0:WINDOW], vals[:, s, j, :], sel[:, s, j, :],
                                                    start=(j == 0), stop=(j == J - 1))
                        last.then_inc(slot_free[s], 1)

                    look_up(0)
                    look_up(1)
                    sum_up(0)
                    look_up(2)
                    sum_up(1)
                    look_up(3)
                    sum_up(2)
                    sum_up(4)
                    sum_up(3)
            pe.wait_ge(all_added, 1)
            by_rest = acc[:, 0:N].rearrange("f (p i) -> f i p", i=NP)
            for n, (i, k) in enumerate(out_parts):
                for q in range(k):
                    last = nc.tensor.matmul(seg[n][0:C, q * H:(q + 1) * H], by_rest[:, i + q, :], w_cols[:],
                                            start=True, stop=True)
                last.then_inc(product, 1)


_INS = ["x", "src", "dst", "edge_attr_64", "edge_weight1", "L0_gnn_W_node", "L0_gnn_W_review"]
_OUTS = [((12500, 16), "float32")]


def kernel(**inputs):
    import numpy as _np
    import concourse.bacc as _bacc
    from concourse import mybir as _mybir
    from concourse.bass_utils import run_bass_kernel_spmd as _run

    nc = _bacc.Bacc("TRN2", target_bir_lowering=False, num_devices=1)
    arrays, args = {}, []
    for name in _INS:
        a = _np.ascontiguousarray(inputs[name])
        arrays[f"in_{name}_dram"] = a
        args.append(nc.dram_tensor(f"in_{name}_dram", a.shape, _mybir.dt.from_np(a.dtype), kind="ExternalInput").ap())
    for i, (shape, dtype) in enumerate(_OUTS):
        dt = _mybir.dt.from_np(_np.dtype(dtype))
        args.append(nc.dram_tensor(f"out_{i}_dram", shape, dt, kind="ExternalOutput").ap())
    bass_gnn_preln(nc, *args)
    r = _run(nc, [arrays], core_ids=[0])
    got = tuple(r.results[0][f"out_{i}_dram"] for i in range(len(_OUTS)))
    return got[0]
```

```python
from contextlib import ExitStack

import concourse.bass as bass
from concourse import mybir

ALU = mybir.AluOpType
ACT = mybir.ActivationFunctionType
AX = mybir.AxisListType
F32 = mybir.dt.float32
I32 = mybir.dt.int32
F16 = mybir.dt.float16

P = 128
J = 5
S = 5
T = S * J
GROUP = J * P
CHUNK = S * GROUP
WINDOW = 64
EPS = 1e-5

PE_TILES = (2, 3, 2, 2, 0)
HALVES = ((0, 1), (2, 3))
ORDER = (0, 1, 2, 4, 3)
G = sum(PE_TILES)
FIRST = [sum(PE_TILES[:s]) for s in range(S)]
NBD = 14
NA = 7
FOUND = 256
DIGIT_B = NA * P
SCALE = 8192.0
ROUNDER = float(3 << 22)


def bass_gnn_preln(
    nc: bass.Bass,
    x: bass.AP,
    src: bass.AP,
    dst: bass.AP,
    edge_attr: bass.AP,
    edge_weight: bass.AP,
    w_node: bass.AP,
    w_review: bass.AP,
    out: bass.AP,
):
    N, H = x.shape
    E, R = edge_attr.shape
    F = R + H
    C = E // CHUNK
    NP = N // C
    assert E == C * CHUNK and C <= P and N == C * NP and F <= P
    assert N <= NBD * DIGIT_B and DIGIT_B <= 2048 and NBD * H <= FOUND
    NPAD = NBD * DIGIT_B

    h_table = nc.dram_tensor("h_table", (NPAD, H), F32, kind="Internal").ap()
    low_dram = nc.dram_tensor("low_dram", (C, G * P), F16, kind="Internal").ap()
    base_dram = nc.dram_tensor("base_dram", (2, C * S), F32, kind="Internal").ap()

    BANK = 512
    QUAD = 4
    parts = [(k, min(QUAD, T - k)) for k in range(0, T, QUAD)]
    high_parts = [(k, min(QUAD, G - k)) for k in range(0, G, QUAD)]
    BLOCK = 32
    QB = NPAD // (4 * BLOCK)
    ROUNDS = 7
    RB = QB // ROUNDS
    assert QB == ROUNDS * RB and RB * BLOCK <= BANK and NPAD <= N + WINDOW and QB <= NP
    LAST = (N - 3 * QB * BLOCK) // BLOCK
    REST = N - (3 * QB + LAST) * BLOCK
    assert 0 < REST and QB - RB < LAST < QB

    def by_blocks(dram, sbuf, low, high):
        for q in range(4):
            end = high if q < 3 else min(high, LAST)
            first = q * QB
            yield (dram[(first + low) * BLOCK:(first + end) * BLOCK, :].rearrange("(k p) f -> p k f", p=BLOCK),
                   sbuf[q * BLOCK:(q + 1) * BLOCK, low:end, :])
        if high == QB:
            yield (dram[N - REST:N, :], sbuf[3 * BLOCK:3 * BLOCK + REST, LAST, :])

    with ExitStack() as ctx:
        def sb(name, shape, dt=F32):
            return ctx.enter_context(nc.sbuf_tensor(name, shape, dt))

        def sem(name):
            return ctx.enter_context(nc.semaphore(name))

        x_sb = sb("x_sb", [C, NP, H])
        rows = sb("rows", [P, NP * H])
        xc = rows[0:C, :].rearrange("p (i f) -> p i f", f=H)
        x_blocks = rows[:, 0:QB * H].rearrange("p (k f) -> p k f", f=H)
        work = sb("work", [P, NP * H])
        sq = work[0:C, :].rearrange("p (i f) -> p i f", f=H)
        h_rows = work[:, 0:NPAD // P * H]
        out_sb = work[:, 0:QB * H].rearrange("p (k f) -> p k f", f=H)
        turned_back = sb("turned_back", [P, 2, RB, BLOCK])
        stat = sb("stat", [C, 4, NP])
        ident = sb("ident", [P, P])
        iota_i = sb("iota_i", [P, WINDOW], I32)
        iota = sb("iota", [P, WINDOW])
        w_rows = sb("w_rows", [H, F])
        w_cols = sb("w_cols", [F, BLOCK])
        arena = sb("arena", [P, 3 * CHUNK])
        src_f = arena[0:C, 0:CHUNK]
        dst_f = arena[0:C, CHUNK:2 * CHUNK]
        wgt_f = arena[0:C, 2 * CHUNK:3 * CHUNK]
        src_i = src_f.bitcast(I32)
        dst_i = dst_f.bitcast(I32)
        hot = []
        at = 0
        for groups in HALVES:
            n = P * sum(PE_TILES[s] for s in groups)
            hot.append(arena[:, at:at + NA * n // 2].bitcast(F16).rearrange("p (a n) -> p a n", a=NA))
            at += NA * n // 2
        span = sb("span", [C, 3, S])
        span_row = sb("span_row", [1, 2, C * S])
        reach = sb("reach", [1, 1])
        reach_i = sb("reach_i", [1, 1], I32)
        base_row = sb("base_row", [1, C * S], I32)
        src_t = sb("src_t", [P, C, T], I32)
        rel_t = sb("rel_t", [P, C, T])
        wgt_t = sb("wgt_t", [P, C, T])
        idx = sb("idx", [P, S, J], I32)
        vals = sb("vals", [P, S, J, F])
        hit = sb("hit", [P, S, J, WINDOW], F16)
        sel = sb("sel", [P, S, J, WINDOW])
        high = sb("high", [C, G * P])
        low = sb("low", [C, G * P], F16)
        low_all = sb("low_all", [P, G * P], F16)
        high_t = sb("high_t", [P, C, G])
        own_i = sb("own_i", [P, NA], I32)
        own = sb("own", [P, NA])
        digit_i = sb("digit_i", [P, NBD], I32)
        digit = sb("digit", [P, NBD])
        table = sb("table", [P, NA, 2, NBD * H], F16)
        by_digit = h_rows.rearrange("p (b a f) -> p a b f", b=NBD, a=NA)
        table_parts = [table[:, :, i, :].rearrange("p a (b f) -> p a b f", f=H) for i in range(2)]
        zeros = sb("zeros", [P, H])
        pick = sb("pick", [P, G, NBD])
        picked_h = sb("picked_h", [P, 2, max(PE_TILES) * NBD * H])
        acc = sb("acc", [F, N + WINDOW])
        banks = [ctx.enter_context(nc.psum_tensor(f"bank{i}", [P, BANK], F32)) for i in range(4)]
        seg = [banks[0], banks[1], banks[2], banks[3], banks[0][:, BANK // 2:BANK]]
        found = [ctx.enter_context(nc.psum_tensor(f"found{i}", [P, 2 * BANK], F32)) for i in range(2)]
        turn = [found[0][:, 0:BANK], found[0][:, BANK:2 * BANK], found[1][:, 0:BANK]]
        result = banks + turn

        x_in = sem("x_in")
        x_again = sem("x_again")
        tail_zero = sem("tail_zero")
        src_in = sem("src_in")
        zeros_made = sem("zeros_made")
        zeros_stored = sem("zeros_stored")
        h_back = sem("h_back")
        low_done = sem("low_done")
        high_done = sem("high_done")
        low_stored = sem("low_stored")
        high_placed = sem("high_placed")
        top_done = sem("top_done")
        table_done = sem("table_done")
        low_in = [sem("low_in_a"), sem("low_in_b")]
        hot_in = [sem("hot_in_a"), sem("hot_in_b")]
        found_in = [sem(f"found_in{s}") for s in range(S)]
        masked = [sem(f"masked{s}") for s in range(S)]
        pick_in = sem("pick_in")
        picked = [sem(f"picked{s}") for s in range(S)]
        hit_in = [sem(f"hit_in{s}") for s in range(S)]
        dst_in = sem("dst_in")
        wgt_in = sem("wgt_in")
        w_in = sem("w_in")
        ident_zero = sem("ident_zero")
        ident_done = sem("ident_done")
        iota_made = sem("iota_made")
        chain = sem("chain")
        var_done = sem("var_done")
        std_done = sem("std_done")
        h_done = sem("h_done")
        h_stored = sem("h_stored")
        src_float = sem("src_float")
        rel_done = sem("rel_done")
        span_done = sem("span_done")
        span_out = sem("span_out")
        span_in = sem("span_in")
        reach_done = sem("reach_done")
        turned = sem("turned")
        src_placed = sem("src_placed")
        rel_placed = sem("rel_placed")
        wgt_placed = sem("wgt_placed")
        w_turned = sem("w_turned")
        w_placed = sem("w_placed")
        ea_in = [sem(f"ea_in{s}") for s in range(S)]
        idx_in = [sem(f"idx_in{s}") for s in range(S)]
        h_in = [sem(f"h_in{s}") for s in range(S)]
        sel_in = [sem(f"sel_in{s}") for s in range(S)]
        slot_free = [sem(f"slot_free{s}") for s in range(S)]
        slots_begun = sem("slots_begun")
        acc_step = sem("acc_step")
        shifted = sem("shifted")
        product = sem("product")
        back_done = sem("back_done")
        out_done = sem("out_done")
        out_stored = sem("out_stored")


        block = ctx.enter_context(nc.Block())

        def columns(half):
            start = FIRST[HALVES[half][0]]
            return slice(P * start, P * (start + sum(PE_TILES[s] for s in HALVES[half])))

        def passes_on(eng):
            eng.wait_ge(reach_done, 1)
            far = eng.value_load(reach_i[0:1, 0:1], min_val=0, max_val=N)
            return far // WINDOW + 1

        @block.sync
        def _(sp):
            sp.dma_start(x_sb[:], x.rearrange("(p i) f -> p i f", p=C)).then_inc(x_in, 16)
            sp.dma_start(src_i, src.rearrange("(c e) -> c e", c=C)).then_inc(src_in, 16)
            sp.dma_start(dst_i, dst.rearrange("(c e) -> c e", c=C)).then_inc(dst_in, 16)
            sp.dma_start(wgt_f, edge_weight.rearrange("(c e) o -> c (e o)", c=C)).then_inc(wgt_in, 16)
            sp.dma_start(w_rows[:, 0:R], w_review).then_inc(w_in, 16)
            sp.dma_start(w_rows[:, R:F], w_node).then_inc(w_in, 16)
            sp.wait_ge(h_done, 1)
            sp.dma_start(h_table[0:N, :].rearrange("(p i) f -> p i f", p=C), xc).then_inc(h_stored, 16)
            sp.wait_ge(zeros_made, 1)
            sp.dma_start(h_table[N:NPAD, :], zeros[0:NPAD - N, :]).then_inc(zeros_stored, 16)
            sp.wait_ge(h_stored, 16)
            sp.wait_ge(zeros_stored, 16)
            sp.dma_start(h_rows.rearrange("p (k f) -> p k f", f=H),
                         h_table.rearrange("(k p) f -> p k f", p=P)).then_inc(h_back, 16)
            sp.wait_ge(span_done, 1)
            sp.dma_start(base_dram.rearrange("k (c s) -> c k s", c=C), span[:, 0:2, :]).then_inc(span_out, 16)
            sp.wait_ge(span_out, 16)
            sp.dma_start(span_row[:], base_dram.rearrange("(o k) g -> o k g", o=1)).then_inc(span_in, 16)
            sp.wait_ge(low_done, 1)
            sp.dma_start(low_dram, low[:]).then_inc(low_stored, 16)
            sp.wait_ge(low_stored, 16)

            def load_low(half, chunk):
                cols = columns(half)
                sp.dma_start(low_all[:, cols], low_dram[bass.ds(chunk, 1), cols].to_broadcast([P, cols.stop - cols.start])
                             ).then_inc(low_in[half], 16)

            load_low(0, 0)
            load_low(1, 0)
            sp.wait_ge(tail_zero, 1)
            for dram, place in by_blocks(x, x_blocks, 0, QB):
                sp.dma_start(place, dram).then_inc(x_again, 16)
            loops = passes_on(sp)
            with sp.Fori(0, loops) as ps:
                with sp.Fori(0, C) as c:
                    turn_no = sp.snap(ps * C + c + 1)
                    for s in ORDER:
                        sp.wait_ge(slot_free[s], turn_no)
                        rows = edge_attr[bass.ds(c * CHUNK + s * GROUP, GROUP), :]
                        sp.dma_start(vals[:, s, :, 0:R], rows.rearrange("(p j) f -> p j f", j=J)).then_inc(ea_in[s], 16)
                    next_chunk = sp.snap((c + 1) % C)
                    for half in range(2):
                        sp.wait_ge(hot_in[half], turn_no)
                        load_low(half, next_chunk)
            for half in range(2):
                sp.wait_ge(low_in[half], loops * (C * 16) + 16)
            stored = 0
            for low_round, high_round in ((0, 3), (3, 6), (6, ROUNDS)):
                sp.wait_ge(out_done, high_round)
                for dram, place in by_blocks(out, out_sb, low_round * RB, high_round * RB):
                    sp.dma_start(dram, place).then_inc(out_stored, 16)
                    stored += 16
            sp.wait_ge(out_stored, stored)

        @block.gpsimd
        def _(pool):
            nc.gpsimd.memset(ident[:], 0.0).then_inc(ident_zero, 1)
            pool.wait_ge(ident_zero, 1)
            nc.gpsimd.affine_select(out=ident[:], in_=ident[:], compare_op=ALU.not_equal, fill=1.0, base=0,
                                    pattern=[[-1, P]], channel_multiplier=1).then_inc(ident_done, 1)
            nc.gpsimd.iota(iota_i[:], pattern=[[1, WINDOW]], base=0, channel_multiplier=0).then_inc(iota_made, 1)
            nc.gpsimd.iota(own_i[:], pattern=[[P, NA]], base=0, channel_multiplier=1).then_inc(iota_made, 1)
            nc.gpsimd.iota(digit_i[:], pattern=[[1, NBD]], base=0, channel_multiplier=0).then_inc(iota_made, 1)
            nc.gpsimd.memset(zeros[:], 0.0).then_inc(zeros_made, 1)
            nc.gpsimd.memset(acc[:], 0.0).then_inc(acc_step, 1)
            pool.wait_ge(h_stored, 16)
            pool.wait_ge(zeros_made, 1)
            pool.wait_ge(iota_made, 3)
            pool.wait_ge(acc_step, 1)
            nc.gpsimd.memset(x_blocks[3 * BLOCK:4 * BLOCK, LAST:QB, :], 0.0).then_inc(tail_zero, 1)
            loops = passes_on(pool)
            with pool.Fori(0, loops) as ps:
                with pool.Fori(0, C) as c:
                    turn_no = pool.snap(ps * C + c + 1)
                    for s in ORDER:
                        pool.wait_ge(idx_in[s], turn_no)
                        pool.sem_inc(slots_begun, 1)
                        for j in range(J - PE_TILES[s]):
                            pool.indirect_dma_start(
                                vals[:, s, j, R:F], None, h_table,
                                bass.IndirectOffsetOnAxis(ap=idx[:, s, j:j + 1], axis=0),
                            ).then_inc(h_in[s], 16)

        @block.scalar
        def _(act):
            act.wait_ge(src_in, 16)
            nc.scalar.copy(src_f, src_i).then_inc(src_float, 1)
            act.wait_ge(var_done, 1)
            nc.scalar.activation(stat[:, 2, :], stat[:, 1, :], ACT.Sqrt).then_inc(std_done, 1)
            for a, (placed, dest) in enumerate(((src_placed, src_t), (wgt_placed, wgt_t), (rel_placed, rel_t))):
                if a == 2:
                    act.wait_ge(h_back, 16)
                    nc.scalar.activation(table_parts[0].rearrange("p a b f -> p b a f"),
                                         h_rows.rearrange("p (b a f) -> p b a f", b=NBD, a=NA),
                                         ACT.Copy, scale=SCALE).then_inc(top_done, 1)
                for i, (k, m) in enumerate(parts):
                    n = a * len(parts) + i
                    act.wait_ge(turned, n + 1)
                    nc.scalar.copy(dest[:, :, k:k + m].rearrange("p c k -> p k c"),
                                   turn[n % 3][:, 0:m * C].rearrange("p (k c) -> p k c", c=C)).then_inc(placed, 1)
            loops = passes_on(act)
            act.wait_ge(src_placed, len(parts))
            act.wait_ge(wgt_placed, len(parts))
            with act.Fori(0, loops) as ps:
                with act.Fori(0, C) as c:
                    turn_no = act.snap(ps * C + c + 1)
                    for s in ORDER:
                        act.wait_ge(slot_free[s], turn_no)
                        nc.scalar.copy(idx[:, s, :], src_t[:, bass.ds(c, 1), s * J:(s + 1) * J].rearrange("p o j -> p (o j)")
                                       ).then_inc(idx_in[s], 1)
                    for s in ORDER:
                        act.wait_ge(hit_in[s], turn_no)
                        for j in range(J):
                            k = s * J + j
                            made = nc.scalar.activation(sel[:, s, j, :], hit[:, s, j, :], ACT.Copy,
                                                        scale=wgt_t[:, bass.ds(c, 1), k:k + 1].rearrange("p o k -> p (o k)"))
                        made.then_inc(sel_in[s], 1)

        @block.vector
        def _(dve):
            steps = [0]

            def link(ins):
                steps[0] += 1
                ins.then_inc(chain, 1)
                dve.wait_ge(chain, steps[0])

            dve.wait_ge(x_in, 16)
            link(nc.vector.tensor_reduce(stat[:, 0, :], x_sb[:], AX.X, ALU.add))
            link(nc.vector.tensor_scalar(stat[:, 1, :], stat[:, 0, :], 1.0 / H, None, ALU.mult))
            link(nc.vector.tensor_tensor(xc, x_sb[:], stat[:, 1, :].unsqueeze(2).to_broadcast([C, NP, H]), ALU.subtract))
            link(nc.vector.tensor_tensor(sq[:], xc, xc, ALU.mult))
            link(nc.vector.tensor_reduce(stat[:, 0, :], sq[:], AX.X, ALU.add))
            nc.vector.tensor_scalar(stat[:, 1, :], stat[:, 0, :], 1.0 / H, EPS, ALU.mult, ALU.add).then_inc(var_done, 1)
            dve.wait_ge(std_done, 1)
            link(nc.vector.reciprocal(stat[:, 3, :], stat[:, 2, :]))
            nc.vector.scalar_tensor_tensor(out=xc, in0=xc, scalar=0.0,
                                           in1=stat[:, 3, :].unsqueeze(2).to_broadcast([C, NP, H]),
                                           op0=ALU.max, op1=ALU.mult).then_inc(h_done, 1)
            dve.wait_ge(dst_in, 16)
            link(nc.vector.tensor_scalar(dst_f, dst_i, float(N), None, ALU.min))
            by_group = dst_f.rearrange("c (s e) -> c s e", s=S)
            link(nc.vector.tensor_reduce(span[:, 0, :], by_group, AX.X, ALU.min))
            link(nc.vector.tensor_reduce(span[:, 2, :], by_group, AX.X, ALU.max))
            nc.vector.tensor_tensor(span[:, 1, :], span[:, 2, :], span[:, 0, :], ALU.subtract).then_inc(span_done, 1)
            nc.vector.tensor_tensor(by_group, by_group, span[:, 0, :].unsqueeze(2).to_broadcast([C, S, GROUP]),
                                    ALU.subtract).then_inc(rel_done, 1)
            dve.wait_ge(iota_made, 1)
            link(nc.vector.tensor_copy(iota[:], iota_i[:]))
            dve.wait_ge(span_in, 16)
            link(nc.vector.tensor_copy(base_row[:], span_row[:, 0, :]))
            link(nc.vector.tensor_reduce(reach[:], span_row[:, 1, :], AX.X, ALU.max))
            nc.vector.tensor_copy(reach_i[:], reach[:]).then_inc(reach_done, 1)
            dve.wait_ge(src_float, 1)
            tiles = src_f.rearrange("c (s p j) -> c s j p", s=S, j=J)
            pe_groups = [(slice(FIRST[s] * P, (FIRST[s] + PE_TILES[s]) * P), tiles[:, s, J - PE_TILES[s]:J, :])
                         for s in range(S) if PE_TILES[s]]
            for cols, of_group in pe_groups:
                last = nc.vector.tensor_scalar(high[:, cols].rearrange("c (g p) -> c g p", p=P), of_group,
                                               1.0 / DIGIT_B, 0.5 / DIGIT_B - 0.5, ALU.mult, ALU.add)
            link(last)
            link(nc.vector.tensor_scalar(high[:], high[:], ROUNDER, None, ALU.add))
            nc.vector.tensor_scalar(high[:], high[:], ROUNDER, None, ALU.subtract).then_inc(high_done, 1)
            dve.wait_ge(high_done, 1)
            for cols, of_group in pe_groups:
                last = nc.vector.scalar_tensor_tensor(out=low[:, cols].rearrange("c (g p) -> c g p", p=P),
                                                      in0=high[:, cols].rearrange("c (g p) -> c g p", p=P),
                                                      scalar=float(-DIGIT_B), in1=of_group, op0=ALU.mult, op1=ALU.add)
            last.then_inc(low_done, 1)
            dve.wait_ge(iota_made, 3)
            link(nc.vector.tensor_copy(own[:], own_i[:]))
            link(nc.vector.tensor_copy(digit[:], digit_i[:]))
            dve.wait_ge(h_back, 16)
            dve.wait_ge(top_done, 1)
            for a in range(NA):
                last = nc.vector.scalar_tensor_tensor(out=table_parts[1][:, a], in0=by_digit[:, a], scalar=SCALE,
                                                      in1=table_parts[0][:, a], op0=ALU.mult, op1=ALU.subtract)
            last.then_inc(table_done, 1)
            for i, (k, m) in enumerate(high_parts):
                n = 3 * len(parts) + i
                dve.wait_ge(turned, n + 1)
                nc.vector.tensor_copy(high_t[:, :, k:k + m].rearrange("p c k -> p k c"),
                                      turn[n % 3][:, 0:m * C].rearrange("p (k c) -> p k c", c=C)).then_inc(high_placed, 1)
            dve.wait_ge(w_turned, 1)
            link(nc.vector.memset(w_cols[:], 0.0))
            nc.vector.tensor_copy(w_cols[:, 0:H], turn[0][0:F, 0:H]).then_inc(w_placed, 1)
            loops = passes_on(dve)
            dve.wait_ge(rel_placed, len(parts))
            dve.wait_ge(high_placed, len(high_parts))

            def make_hot(half):
                for a in range(NA):
                    made = nc.vector.tensor_scalar(hot[half][:, a, :], low_all[:, columns(half)], own[:, a:a + 1],
                                                   None, ALU.is_equal)
                made.then_inc(hot_in[half], 1)

            dve.wait_ge(turned, 3 * len(parts) + len(high_parts))
            dve.wait_ge(low_in[0], 16)
            make_hot(0)
            with dve.Fori(0, loops) as ps:
                with dve.Fori(0, C) as c:
                    turn_no = dve.snap(ps * C + c + 1)
                    step = dve.snap((ps * C + c) * S + 1)
                    dve.wait_ge(acc_step, step)
                    nc.vector.tensor_tensor(pick[:], high_t[:, bass.ds(c, 1), :].rearrange("p o g -> p (o g)").unsqueeze(2).to_broadcast([P, G, NBD]),
                                            digit[:].unsqueeze(1).to_broadcast([P, G, NBD]), ALU.is_equal).then_inc(pick_in, 1)
                    for s in ORDER:
                        dve.wait_ge(slot_free[s], turn_no)
                        nc.vector.tensor_tensor(hit[:, s], iota[:].unsqueeze(1).to_broadcast([P, J, WINDOW]),
                                                rel_t[:, bass.ds(c, 1), s * J:(s + 1) * J].rearrange("p o j -> p (o j)").unsqueeze(2).to_broadcast([P, J, WINDOW]),
                                                ALU.is_equal).then_inc(hit_in[s], 1)

                    def choose(s):
                        m = PE_TILES[s]
                        dve.wait_ge(found_in[s], turn_no)
                        dve.wait_ge(pick_in, turn_no)
                        if s >= 2:
                            dve.wait_ge(picked[s - 2], turn_no)
                        nc.vector.scalar_tensor_tensor(
                            out=picked_h[:, s % 2, 0:m * NBD * H].rearrange("p (g b f) -> p g b f", g=m, b=NBD),
                            in0=found[s % 2][:].rearrange("p (g n) -> p g n", n=FOUND)[:, 0:m, 0:NBD * H].rearrange("p g (b f) -> p g b f", b=NBD),
                            scalar=1.0 / SCALE,
                            in1=pick[:, FIRST[s]:FIRST[s] + m, :].unsqueeze(3).to_broadcast([P, m, NBD, H]),
                            op0=ALU.mult, op1=ALU.mult).then_inc(masked[s], 1)
                        dve.wait_ge(masked[s], turn_no)
                        nc.vector.tensor_reduce(vals[:, s, J - m:J, R:F],
                                                picked_h[:, s % 2, 0:m * NBD * H].rearrange("p (g b f) -> p g f b", g=m, b=NBD),
                                                AX.X, ALU.add).then_inc(picked[s], 1)

                    def add_up(n):
                        s = ORDER[n]
                        base = dve.value_load(base_row[0:1, bass.ds(c * S + s, 1)], min_val=0, max_val=N)
                        dve.wait_ge(slot_free[s], turn_no + 1)
                        dve.wait_ge(acc_step, step + n)
                        window = acc[:, bass.ds(base, WINDOW)]
                        nc.vector.tensor_tensor(window, window, seg[s][0:F, 0:WINDOW], ALU.add).then_inc(acc_step, 1)

                    choose(0)
                    dve.wait_ge(low_in[1], turn_no * 16)
                    make_hot(1)
                    choose(1)
                    add_up(0)
                    dve.wait_ge(low_in[0], turn_no * 16 + 16)
                    make_hot(0)
                    choose(2)
                    add_up(1)
                    choose(3)
                    add_up(2)
                    add_up(3)
                    add_up(4)
                nc.vector.tensor_scalar(rel_t[:], rel_t[:], float(WINDOW), None, ALU.subtract).then_inc(shifted, 1)
                nc.vector.tensor_scalar(base_row[:], base_row[:], float(WINDOW), float(N), ALU.add, ALU.min).then_inc(shifted, 1)
                dve.wait_ge(shifted, ps * 2 + 2)
            dve.wait_ge(x_again, 16 * 5)
            for r in range(ROUNDS):
                dve.wait_ge(product, r + 1)
                back = turned_back[:, r % 2]
                if r >= 2:
                    dve.wait_ge(out_done, r - 1)
                nc.vector.transpose(back.rearrange("p k f -> p (k f)"), result[r][:, 0:RB * BLOCK]).then_inc(back_done, 1)
                dve.wait_ge(back_done, r + 1)
                blocks = slice(r * RB, (r + 1) * RB)
                nc.vector.tensor_tensor(out_sb[:, blocks, :], back[:, :, 0:H], x_blocks[:, blocks, :],
                                        ALU.add).then_inc(out_done, 1)

        @block.tensor
        def _(pe):
            pe.wait_ge(ident_done, 1)
            for s in range(S):
                pe.sem_inc(slot_free[s], 1)
            n = 0
            by_tile = [a.rearrange("c (s p j) -> c s j p", s=S, j=J) for a in (src_f, wgt_f, dst_f)]
            by_tile = [[a[:, k // J, k % J, :] for k in range(T)] for a in by_tile]
            by_tile.append([high[:, g * P:(g + 1) * P] for g in range(G)])
            for tiles, ready, count in zip(by_tile, (src_float, wgt_in, rel_done, high_done), (1, 16, 1, 1)):
                pe.wait_ge(ready, count)
                for k, m in (parts if len(tiles) == T else high_parts):
                    if n >= 3:
                        a, i = divmod(n - 3, len(parts))
                        pe.wait_ge((src_placed, wgt_placed, rel_placed)[a], i + 1)
                    for q in range(m):
                        last = nc.tensor.transpose(turn[n % 3][:, q * C:(q + 1) * C], tiles[k + q], ident[0:C, 0:C])
                    last.then_inc(turned, 1)
                    n += 1
            pe.wait_ge(high_placed, len(high_parts))
            pe.wait_ge(w_in, 32)
            nc.tensor.transpose(turn[0][0:F, 0:H], w_rows[:], ident[0:H, 0:H]).then_inc(w_turned, 1)
            loops = passes_on(pe)
            pe.wait_ge(table_done, 1)
            pe.wait_ge(w_placed, 1)
            with pe.Fori(0, loops) as ps:
                with pe.Fori(0, C) as c:
                    turn_no = pe.snap(ps * C + c + 1)

                    def look_up(s):
                        half = s // 2
                        if s == HALVES[half][0]:
                            pe.wait_ge(hot_in[half], turn_no)
                        for a in range(NA):
                            for g in range(PE_TILES[s]):
                                at = (FIRST[s] + g) * P - columns(half).start
                                for part in range(2):
                                    last = nc.tensor.matmul(found[s % 2][:, g * FOUND:g * FOUND + NBD * H],
                                                            hot[half][:, a, at:at + P], table[:, a, part, :],
                                                            start=(a == 0 and g % 2 == 0 and part == 0),
                                                            stop=(a == NA - 1 and part == 1), skip_group_check=True)
                        last.then_inc(found_in[s], 1)

                    def sum_up(s):
                        pe.wait_ge(sel_in[s], turn_no)
                        pe.wait_ge(ea_in[s], turn_no * 16)
                        pe.wait_ge(h_in[s], turn_no * (16 * (J - PE_TILES[s])))
                        if PE_TILES[s]:
                            pe.wait_ge(picked[s], turn_no)
                        for j in range(J):
                            last = nc.tensor.matmul(seg[s][0:F, 0:WINDOW], vals[:, s, j, :], sel[:, s, j, :],
                                                    start=(j == 0), stop=(j == J - 1))
                        last.then_inc(slot_free[s], 1)

                    look_up(0)
                    look_up(1)
                    sum_up(0)
                    look_up(2)
                    sum_up(1)
                    look_up(3)
                    sum_up(2)
                    sum_up(4)
                    sum_up(3)
            pe.wait_ge(acc_step, loops * (C * S) + 1)
            for r in range(ROUNDS):
                for q in range(4):
                    first = (q * QB + r * RB) * BLOCK
                    last = nc.tensor.matmul(result[r][q * BLOCK:(q + 1) * BLOCK, 0:RB * BLOCK], w_cols[:],
                                            acc[:, first:first + RB * BLOCK], start=True, stop=True,
                                            tile_position=(0, q * BLOCK))
                last.then_inc(product, 1)


_INS = ["x", "src", "dst", "edge_attr_64", "edge_weight1", "L0_gnn_W_node", "L0_gnn_W_review"]
_OUTS = [((12500, 16), "float32")]


def kernel(**inputs):
    import numpy as _np
    import concourse.bacc as _bacc
    from concourse import mybir as _mybir
    from concourse.bass_utils import run_bass_kernel_spmd as _run

    nc = _bacc.Bacc("TRN2", target_bir_lowering=False, num_devices=1)
    arrays, args = {}, []
    for name in _INS:
        a = _np.ascontiguousarray(inputs[name])
        arrays[f"in_{name}_dram"] = a
        args.append(nc.dram_tensor(f"in_{name}_dram", a.shape, _mybir.dt.from_np(a.dtype), kind="ExternalInput").ap())
    for i, (shape, dtype) in enumerate(_OUTS):
        dt = _mybir.dt.from_np(_np.dtype(dtype))
        args.append(nc.dram_tensor(f"out_{i}_dram", shape, dt, kind="ExternalOutput").ap())
    bass_gnn_preln(nc, *args)
    r = _run(nc, [arrays], core_ids=[0])
    got = tuple(r.results[0][f"out_{i}_dram"] for i in range(len(_OUTS)))
    return got[0]
```
